# Optimizing a Trainium2 kernel written in Bass

```python
import numpy as np
import jax
import jax.numpy as jnp

def _softmax(x, axis=-1):
    return jax.nn.softmax(x, axis=axis)

def _gelu(x):
    return jax.nn.gelu(x, approximate=True)

def _silu(x):
    return jax.nn.silu(x)

def _sigmoid(x):
    return jax.nn.sigmoid(x)

def _layernorm(x, axis=-1, eps=1e-05):
    m = jnp.mean(x, axis=axis, keepdims=True)
    v = jnp.var(x, axis=axis, keepdims=True)
    return (x - m) / jnp.sqrt(v + eps)

def _scatter_add(tgt, idx, src, axis=0):
    return tgt.at[idx].add(src)

def _segment_sum(src, seg, n):
    return jax.ops.segment_sum(src, seg, n)
kernel_name = 'mk_flamingo_gated_d2_seqx_r4_698d0b'

def setup_inputs(seed: int=0):
    np.random.seed(seed)
    _w = jnp.asarray

    def _rec_inputs():
        import jax
        import jax.numpy as jnp
        _rk = jax.random.key(seed)
        x = 7.22e-05 + 1 * jax.random.normal(jax.random.fold_in(_rk, 1), (32, 112, 256), jnp.float32)
        _lenS = 112 - jax.random.randint(jax.random.fold_in(_rk, 7), (32,), 0, max(1, 112 // 4) + 1, jnp.int32)
        _lenS2 = 375 - jax.random.randint(jax.random.fold_in(_rk, 8), (32,), 0, max(1, 375 // 4) + 1, jnp.int32)
        _ctx_768P = jax.random.normal(jax.random.fold_in(_rk, 11), (32, 16, 192), jnp.float32)
        _ctx_768c = jax.random.dirichlet(jax.random.fold_in(_rk, 511), 0.3 * jnp.ones((16,), jnp.float32), (32, 375))
        _ctx_768t = jnp.einsum('bsk,bkd->bsd', _ctx_768c, _ctx_768P)
        _ctx_768t = _ctx_768t * jax.lax.rsqrt(jnp.mean(jnp.square(_ctx_768t)) + 1e-12) * 0.953939
        ctx_768 = -0.000191848 + 0.999787 * (_ctx_768t + 0.3 * jax.random.normal(jax.random.fold_in(_rk, 611), (32, 375, 192), jnp.float32))
        _g = jax.random.normal(jax.random.fold_in(_rk, 9001), (2, 2), jnp.float32)
        _g = jnp.sign(_g) * jnp.maximum(jnp.abs(_g), 1.0) + (_g == 0) * 1.0
        g_xattn = _g[0]
        g_ffn = _g[1]
        return (x, ctx_768, g_xattn, g_ffn)
    x, ctx_768, g_xattn, g_ffn = _rec_inputs()

    def _L0_xattn_setup():
        import jax, jax.numpy as jnp
        import numpy as np
        DIM_Q = 256
        DIM_KV = 192
        N_HEADS = 4

        def _split_heads(x):
            b, l, d = x.shape
            return x.reshape(b, l, N_HEADS, d // N_HEADS).transpose(0, 2, 1, 3)
        key = jax.random.key(seed)
        ks = jax.random.split(key, 7)
        b, lq, lkv = (4, 512, 512)
        q = jax.random.normal(ks[0], (b, lq, DIM_Q), dtype=jnp.float32)
        kv = jax.random.normal(ks[1], (b, lkv, DIM_KV), dtype=jnp.float32)
        s_q = 1.0 / np.sqrt(DIM_Q)
        s_kv = 1.0 / np.sqrt(DIM_KV)
        Wq = jax.random.normal(ks[2], (DIM_Q, DIM_Q), dtype=jnp.float32) * s_q
        Wk = jax.random.normal(ks[3], (DIM_Q, DIM_KV), dtype=jnp.float32) * s_kv
        Wv = jax.random.normal(ks[4], (DIM_Q, DIM_KV), dtype=jnp.float32) * s_kv
        Wo = jax.random.normal(ks[5], (DIM_Q, DIM_Q), dtype=jnp.float32) * s_q
        bo = jax.random.normal(ks[6], (DIM_Q,), dtype=jnp.float32) * 0.01
        return {'q': q, 'kv': kv, 'Wq': Wq, 'Wk': Wk, 'Wv': Wv, 'Wo': Wo, 'bo': bo}
    _L0_xattn_all = _L0_xattn_setup()
    _L0_xattn_in = {k: v for k, v in _L0_xattn_all.items() if k in ('Wq', 'Wk', 'Wv', 'Wo', 'bo')}
    del _L0_xattn_all

    def _L0_ffn_setup():
        import jax, jax.numpy as jnp
        import numpy as np
        ALPHA = 1.0
        key = jax.random.key(seed)
        ks = jax.random.split(key, 7)
        B, S, IN, OUT = (8, 2048, 256, 256)
        RANK, DDIM, UDIM = (4, 100, 50)
        return {'hidden_states': jax.random.normal(ks[0], (B, S, IN), dtype=jnp.float32), 'W': jax.random.normal(ks[1], (OUT, IN), dtype=jnp.float32) * 0.02, 'b': jax.random.normal(ks[2], (OUT,), dtype=jnp.float32) * 0.02, 'lora_down': jax.random.normal(ks[3], (RANK, DDIM), dtype=jnp.float32) * 0.1, 'lora_up': jax.random.normal(ks[4], (UDIM, RANK), dtype=jnp.float32) * 0.1, 'down_aux': jax.random.normal(ks[5], (DDIM, IN), dtype=jnp.float32) * 0.03, 'up_aux': jax.random.normal(ks[6], (OUT, UDIM), dtype=jnp.float32) * 0.03}
    _L0_ffn_all = _L0_ffn_setup()
    _L0_ffn_in = {k: v for k, v in _L0_ffn_all.items() if k in ('W', 'b', 'lora_down', 'lora_up', 'down_aux', 'up_aux')}
    del _L0_ffn_all

    def _L1_xattn_setup():
        import jax, jax.numpy as jnp
        import numpy as np
        B, LQ, LK = (4, 512, 512)
        D1, D2, H = (256, 192, 256)
        key = jax.random.key(seed)
        ks = jax.random.split(key, 9)
        s1, s2, sh = (1.0 / np.sqrt(D1), 1.0 / np.sqrt(D2), 1.0 / np.sqrt(H))
        return {'query': jax.random.normal(ks[0], (B, LQ, D1), jnp.float32), 'key': jax.random.normal(ks[1], (B, LK, D2), jnp.float32), 'value': jax.random.normal(ks[2], (B, LK, D2), jnp.float32), 'Wq': jax.random.normal(ks[3], (D1, H), jnp.float32) * s1, 'bq': jax.random.normal(ks[4], (H,), jnp.float32) * s1, 'Wk': jax.random.normal(ks[5], (D2, H), jnp.float32) * s2, 'bk': jax.random.normal(ks[6], (H,), jnp.float32) * s2, 'Wv': jax.random.normal(ks[7], (D2, H), jnp.float32) * s2, 'bv': jax.random.normal(ks[8], (H,), jnp.float32) * s2}
    _L1_xattn_all = _L1_xattn_setup()
    _L1_xattn_in = {k: v for k, v in _L1_xattn_all.items() if k in ('Wq', 'bq', 'Wk', 'bk', 'Wv', 'bv')}
    del _L1_xattn_all

    def _L1_ffn_setup():
        import jax, jax.numpy as jnp
        import numpy as np
        NUM_HEADS = 16
        TOP_K = 2
        key = jax.random.key(seed)
        ks = jax.random.split(key, 5)
        B, S, D, E = (4, 512, 256, 8)
        scale = 0.02
        return {'x': jax.random.normal(ks[0], (B, S, D), dtype=jnp.float32), 'W_qkv': jax.random.normal(ks[1], (D, 3 * D), dtype=jnp.float32) * scale, 'b_qkv': jnp.zeros((3 * D,), dtype=jnp.float32), 'W_gate': jax.random.normal(ks[2], (D, E), dtype=jnp.float32) * scale, 'b_gate': jnp.zeros((E,), dtype=jnp.float32), 'W_experts': jax.random.normal(ks[3], (E, D, D), dtype=jnp.float32) * scale, 'b_experts': jnp.zeros((E, D), dtype=jnp.float32)}
    _L1_ffn_all = _L1_ffn_setup()
    _L1_ffn_in = {k: v for k, v in _L1_ffn_all.items() if k in ('W_qkv', 'b_qkv', 'W_gate', 'b_gate', 'W_experts', 'b_experts')}
    del _L1_ffn_all
    return {'x': x, 'ctx_768': ctx_768, 'g_xattn': g_xattn, 'g_ffn': g_ffn, 'L0_xattn_Wq': _L0_xattn_in['Wq'], 'L0_xattn_Wk': _L0_xattn_in['Wk'], 'L0_xattn_Wv': _L0_xattn_in['Wv'], 'L0_xattn_Wo': _L0_xattn_in['Wo'], 'L0_xattn_bo': _L0_xattn_in['bo'], 'L0_ffn_W': _L0_ffn_in['W'], 'L0_ffn_b': _L0_ffn_in['b'], 'L0_ffn_lora_down': _L0_ffn_in['lora_down'], 'L0_ffn_lora_up': _L0_ffn_in['lora_up'], 'L0_ffn_down_aux': _L0_ffn_in['down_aux'], 'L0_ffn_up_aux': _L0_ffn_in['up_aux'], 'L1_xattn_Wq': _L1_xattn_in['Wq'], 'L1_xattn_bq': _L1_xattn_in['bq'], 'L1_xattn_Wk': _L1_xattn_in['Wk'], 'L1_xattn_bk': _L1_xattn_in['bk'], 'L1_xattn_Wv': _L1_xattn_in['Wv'], 'L1_xattn_bv': _L1_xattn_in['bv'], 'L1_ffn_W_qkv': _L1_ffn_in['W_qkv'], 'L1_ffn_b_qkv': _L1_ffn_in['b_qkv'], 'L1_ffn_W_gate': _L1_ffn_in['W_gate'], 'L1_ffn_b_gate': _L1_ffn_in['b_gate'], 'L1_ffn_W_experts': _L1_ffn_in['W_experts'], 'L1_ffn_b_experts': _L1_ffn_in['b_experts']}

def reference(x, ctx_768, g_xattn, g_ffn, L0_xattn_Wq, L0_xattn_Wk, L0_xattn_Wv, L0_xattn_Wo, L0_xattn_bo, L0_ffn_W, L0_ffn_b, L0_ffn_lora_down, L0_ffn_lora_up, L0_ffn_down_aux, L0_ffn_up_aux, L1_xattn_Wq, L1_xattn_bq, L1_xattn_Wk, L1_xattn_bk, L1_xattn_Wv, L1_xattn_bv, L1_ffn_W_qkv, L1_ffn_b_qkv, L1_ffn_W_gate, L1_ffn_b_gate, L1_ffn_W_experts, L1_ffn_b_experts):
    import jax
    import jax.numpy as jnp

    def _L0_xattn_ref(q, kv, Wq, Wk, Wv, Wo, bo):
        import jax, jax.numpy as jnp
        import numpy as np
        DIM_Q = 256
        DIM_KV = 192
        N_HEADS = 4

        def _split_heads(x):
            b, l, d = x.shape
            return x.reshape(b, l, N_HEADS, d // N_HEADS).transpose(0, 2, 1, 3)
        qp = q @ Wq.T
        kp = kv @ Wk.T
        vp = kv @ Wv.T
        qh, kh, vh = (_split_heads(qp), _split_heads(kp), _split_heads(vp))
        scale = (DIM_Q // N_HEADS) ** (-0.5)
        scores = jnp.einsum('bhqd,bhkd->bhqk', qh, kh) * scale
        attn = jax.nn.softmax(scores, axis=-1)
        ctx = jnp.einsum('bhqk,bhkd->bhqd', attn, vh)
        b, h, lq, hd = ctx.shape
        ctx = ctx.transpose(0, 2, 1, 3).reshape(b, lq, h * hd)
        return ctx @ Wo.T + bo

    def _L0_ffn_ref(hidden_states, W, b, lora_down, lora_up, down_aux, up_aux):
        import jax, jax.numpy as jnp
        import numpy as np
        ALPHA = 1.0
        lilora_weight = up_aux @ (lora_up @ (lora_down @ down_aux))
        base = jnp.einsum('bsi,oi->bso', hidden_states, W) + b
        delta = jnp.einsum('bsi,oi->bso', hidden_states, lilora_weight)
        return base + ALPHA * delta

    def _L1_xattn_ref(query, key, value, Wq, bq, Wk, bk, Wv, bv):
        import jax, jax.numpy as jnp
        import numpy as np
        B, LQ, LK = (4, 512, 512)
        D1, D2, H = (256, 192, 256)
        q = jnp.einsum('bqd,dh->bqh', query, Wq) + bq
        k = jnp.einsum('bkd,dh->bkh', key, Wk) + bk
        v = jnp.einsum('bkd,dh->bkh', value, Wv) + bv
        scores = jnp.einsum('bqh,bkh->bqk', q, k)
        weights = jax.nn.softmax(scores, axis=-1)
        return jnp.einsum('bqk,bkh->bqh', weights, v)

    def _L1_ffn_ref(x, W_qkv, b_qkv, W_gate, b_gate, W_experts, b_experts):
        import jax, jax.numpy as jnp
        import numpy as np
        NUM_HEADS = 16
        TOP_K = 2
        B, S, D = x.shape
        H = NUM_HEADS
        hd = D // H
        E = W_gate.shape[-1]
        qkv = (x @ W_qkv + b_qkv).reshape(B, S, 3, H, hd)
        q, k, v = (qkv[:, :, 0], qkv[:, :, 1], qkv[:, :, 2])
        attn = jnp.einsum('bqhd,bkhd->bhqk', q, k) / jnp.sqrt(jnp.asarray(hd, x.dtype))
        attn = jax.nn.softmax(attn, axis=-1)
        attn_out = jnp.einsum('bhqk,bkhd->bqhd', attn, v).reshape(B, S, D)
        gate = jax.nn.softmax(x @ W_gate + b_gate, axis=-1)
        top_g, top_i = jax.lax.top_k(gate, TOP_K)
        combine = jnp.sum(jax.nn.one_hot(top_i, E, dtype=x.dtype) * top_g[..., None], axis=2)
        expert_out = jnp.einsum('bsd,edf->bsef', x, W_experts) + b_experts
        moe_out = jnp.einsum('bsef,bse->bsf', expert_out, combine)
        return attn_out + moe_out
    x = x + jnp.tanh(g_xattn[0]) * _L0_xattn_ref(_layernorm(x, axis=-1), ctx_768, L0_xattn_Wq, L0_xattn_Wk, L0_xattn_Wv, L0_xattn_Wo, L0_xattn_bo)
    x = x + jnp.tanh(g_ffn[0]) * _L0_ffn_ref(_layernorm(x, axis=-1), L0_ffn_W, L0_ffn_b, L0_ffn_lora_down, L0_ffn_lora_up, L0_ffn_down_aux, L0_ffn_up_aux)
    x = x + jnp.tanh(g_xattn[1]) * _L1_xattn_ref(_layernorm(x, axis=-1), ctx_768, ctx_768, L1_xattn_Wq, L1_xattn_bq, L1_xattn_Wk, L1_xattn_bk, L1_xattn_Wv, L1_xattn_bv)
    x = x + jnp.tanh(g_ffn[1]) * _L1_ffn_ref(_layernorm(x, axis=-1), L1_ffn_W_qkv, L1_ffn_b_qkv, L1_ffn_W_gate, L1_ffn_b_gate, L1_ffn_W_experts, L1_ffn_b_experts)
    return x

_drawn_inputs = setup_inputs


def setup_inputs(seed=0):
    import zlib

    import numpy as np

    out = dict(_drawn_inputs(seed))
    spreads = {'g_ffn': (-1.0, 0.6),
     'L1_ffn_b_qkv': (0.0, 0.1),
     'L1_ffn_b_gate': (0.0, 0.357),
     'L1_ffn_b_experts': (0.0, 0.621)}
    factors = {'L0_xattn_bo': 3.708, 'L1_xattn_bk': 8.0}
    for name, (base, spread) in spreads.items():
        noise = np.random.default_rng([zlib.crc32(name.encode()), seed]).standard_normal(out[name].shape)
        drawn = base * np.exp(spread * noise) if base else spread * noise
        out[name] = jnp.asarray(drawn.astype(out[name].dtype))
    for name, factor in factors.items():
        out[name] = (out[name] * factor).astype(out[name].dtype)
    return out
```

```python
from contextlib import ExitStack

import concourse.bass as bass
from concourse import mybir

F32 = mybir.dt.float32
F16 = mybir.dt.float16
U32 = mybir.dt.uint32
ALU = mybir.AluOpType
ACT = mybir.ActivationFunctionType
AX = mybir.AxisListType

P = 128
SX = 16.0
SW = 256.0
SP = 1024.0
SZ = 4.0
EPS = 1e-5
DMA = 16
PEEL = 4




class Chain:

    def __init__(self, sem, steps, by=1):
        self.sem, self.steps, self.by = sem, steps.split(), by

    def after(self, step, b):
        return b * (self.by * len(self.steps)) + self.by * (self.steps.index(step) + 1)


def past(b):
    return not (isinstance(b, int) and b < 0)


def flamingo_kernel(nc, x, ctx_dup, consts, gates, bias_rows, w_lin, lora_downT, down_aux, lora_upT, up_auxT,
                    w_l1qT, w_l1kT, b_l1q, w_qk, w_vg, b_stack, w_exp, b_exp, out):
    NB, LQ, D = x.shape
    _, LKP, NKC, DUP = ctx_dup.shape
    LK = LKP * NKC
    KD = D // P
    H0, HD0 = 4, D // 4
    H1, HD1 = 16, D // 16
    E = w_exp.shape[2]
    NG = 4
    HG = H1 // NG

    with ExitStack() as ctx:
        def sb(name, shape, dt=F32):
            return ctx.enter_context(nc.sbuf_tensor(name, shape, dt))

        def pair(name, shape):
            return sb(name + "_hi", shape, F16), sb(name + "_lo", shape, F16)

        def chain(name, steps, by=1):
            return Chain(ctx.enter_context(nc.semaphore(name)), steps, by)

        def sem(name):
            return ctx.enter_context(nc.semaphore(name))

        bank = [ctx.enter_context(nc.psum_tensor(f"bank{n}", [P, 512], F32)) for n in range(8)]

        cst = sb("cst", list(consts.shape))
        ident = cst[:, 0:P]
        keep_hi_row = cst[0:2, P:P + 1]
        parity = cst[:, P + 1:P + 3]
        iota = cst[0:LQ, P + 3:P + 3 + E]
        minus_half = cst[0:LQ, P + 3 + E:P + 4 + E]
        ones16 = sb("ones16", [2, LQ], F16)
        gate_in = sb("gate_in", [LQ, 4])
        th = sb("th", [LQ, 4])
        gsc = sb("gsc", [LQ, 6])
        brow = sb("brow", [LQ, 3, D])
        gbrow = sb("gbrow", [LQ, 3, D])
        lin = sb("lin", [P, 6, KD, D])
        lin_hi, lin_lo = pair("linw", [P, 6, KD, D])
        WQ, WK, WV, WO, WF, WV1 = range(6)
        ldT, dax = sb("ldT", list(lora_downT.shape)), sb("dax", list(down_aux.shape))
        luT, uaT = sb("luT", list(lora_upT.shape)), sb("uaT", list(up_auxT.shape))
        RANK, DDIM, UDIM = lora_upT.shape[0], down_aux.shape[0], up_auxT.shape[0]
        t1 = sb("t1", [RANK, D])
        t2 = sb("t2", [UDIM, D])
        l1q, l1k = sb("l1q", [P, KD, D]), sb("l1k", [P, KD, D + 1])
        l1b = sb("l1b", [P, KD, 2])
        A_hi, A_lo = pair("A", [P, KD, D + 1])
        NQK, NVG = 2 * D, D + E
        wqk, wvg = sb("wqk", [P, KD, NQK]), sb("wvg", [P, KD, NVG])
        wqk_hi, wqk_lo = pair("wqks", [P, KD, NQK])
        wvg_hi, wvg_lo = pair("wvgs", [P, KD, NVG])
        NST = D + 1 + NQK + NVG
        stack_f = sb("stack_f", [2, NST])
        stack_h = sb("stack_h", [2, NST], F16)
        stack = sb("stack", [2, NST], F16)
        b_A = stack[:, 0:D + 1]
        b_qk = stack[:, D + 1:D + 1 + NQK]
        b_vg = stack[:, D + 1 + NQK:NST]
        wex = sb("wex", [P, KD, E, D])
        wex_hi, wex_lo = pair("wexs", [P, KD, E, D])
        bex = sb("bex", [E, D])

        cinS = sb("cinS", [LKP, NKC, DUP])
        cin = sb("cin", [LKP, NKC, DUP])
        NKV = 3 * LK + 2 * NKC * DUP
        kv = [sb(f"kv{g}", [P, NKV], F16) for g in "ABC"]

        def kvT0_hi(g): return kv[g][:, 0:LK]
        def kvT0_lo(g): return kv[g][:, LK:2 * LK]
        def kvT1(g): return kv[g][:, 2 * LK:3 * LK]
        def kvn(g, part):
            o = 3 * LK + part * NKC * DUP
            return kv[g][0:LKP, o:o + NKC * DUP].rearrange("p (c d) -> p c d", c=NKC)

        k_hi, k_lo = pair("k", [P, KD, LK])
        v_hi, v_lo = pair("v", [LKP, NKC, H0, HD0 + 1])

        xin, xg = sb("xin", [LQ, D]), sb("xg", [LQ, D])
        x1, x1g = sb("x1", [LQ, D]), sb("x1g", [LQ, D])
        x2, x2g = sb("x2", [LQ, D]), sb("x2g", [LQ, D])
        x3, acc, xout = sb("x3", [LQ, D]), sb("acc", [LQ, D]), sb("xout", [LQ, D])
        ln_st = [sb(f"ln{n}_st", [LQ, 6]) for n in range(4)]
        ln_mv = [sb(f"ln{n}_mv", [LQ, 2]) for n in range(4)]
        ln_ve = [sb(f"ln{n}_ve", [LQ, 1]) for n in range(4)]
        ln_sh = [sb(f"ln{n}_sh", [LQ, 1]) for n in range(4)]
        ln_rs = [sb(f"ln{n}_rs", [LQ, 1]) for n in range(4)]
        xn = [sb(f"xn{n}", [LQ, D]) for n in range(4)]
        xT = [pair(f"xT{n}", [P, KD, LQ]) for n in range(4)]

        q_hi, q_lo = pair("q", [P, KD, LQ])
        mx0, nb0 = sb("mx0", [LQ, H0]), sb("nb0", [LQ, H0])
        p0 = sb("p0", [LQ, H0, LK])
        p0T_hi, p0T_lo = pair("p0T", [LKP, H0, NKC, P])
        rec0, o0 = sb("rec0", [LQ, H0]), sb("o0", [LQ, D])
        oT_hi, oT_lo = pair("oT", [P, KD, LQ])

        qp_hi, qp_lo = pair("qp", [P, KD, LQ])
        qc = sb("qc", [LQ, 1])
        mx1, mm1, nb1, rs1 = (sb(n, [LQ, 1]) for n in ("mx1", "mm1", "nb1", "rs1"))
        rr1, gr1 = sb("rr1", [LQ, 1]), sb("gr1", [LQ, 1])
        p1 = sb("p1", [LQ, LK])
        p1T_hi, p1T_lo = pair("p1T", [LKP, NKC, LQ])
        z_hi, z_lo = sb("z_hi", [P, KD, LQ], F16), sb("z_lo", [P, LQ], F16)

        q2_hi, q2_lo = pair("q2", [P, KD, LQ])
        k2_hi, k2_lo = pair("k2", [P, KD, 2, LQ])
        v2_hi, v2_lo = pair("v2", [LQ, H1, HD1 + 1])
        mg, ng, eg, sg = sb("mg", [LQ, 1]), sb("ng", [LQ, 1]), sb("eg", [LQ, E]), sb("sg", [LQ, 1])
        top, topi, topf = sb("top", [LQ, 8]), sb("topi", [LQ, 8], U32), sb("topf", [LQ, 2])
        pick0, pick1, comb = sb("pick0", [LQ, E]), sb("pick1", [LQ, E]), sb("comb", [LQ, E])
        rsg, cgS, cgb, cT = sb("rsg", [LQ, 1]), sb("cgS", [LQ, E]), sb("cgb", [LQ, E]), sb("cT", [E, LQ])
        mx2, nb2 = sb("mx2", [LQ, H1]), sb("nb2", [LQ, H1])
        p2 = sb("p2", [LQ, H1, LQ])
        p2T_hi, p2T_lo = pair("p2T", [LQ, H1, P])
        rec2, o2 = sb("rec2", [LQ, H1]), sb("o2", [LQ, D])
        part = sb("part", [LQ, E, D])

        def slot_head(s):
            c, r = divmod(s, 8)
            g, r = divmod(r, 4)
            return 8 * c + [0, 1, 4, 5][r] + 2 * g

        loads = [sem(n) for n in ("consts_loaded", "linear_loaded", "lora_loaded", "layer1_loaded", "ffn1_loaded",
                                  "experts_loaded")]
        prep, prep_pe, prep_act, prep_pool = sem("prep_dve"), sem("prep_pe"), sem("prep_act"), sem("prep_pool")
        ctx_in = chain("ctx_in", "c", DMA)
        x_in = chain("x_in", "x", DMA)
        copyAB = chain("copyAB", "c", DMA)
        copyBC = chain("copyBC", "c", DMA)
        stored = chain("stored", "c", DMA)
        kvT = [chain(f"kvT{n}", "ps hi lo") for n in range(2)]
        kvn_split = chain("kvn_split", "scaled hi lo")
        kproj = [chain(f"kproj{n}", "ps hi lo") for n in range(2)]
        vproj = [chain(f"vproj{n}", "ps hi lo") for n in range(2)]
        ln = [chain(f"ln{n}", "stats mean_var var_eps rstd shift xn") for n in range(4)]
        xTs = [chain(f"xT{n}s", "ps hi lo") for n in range(4)]
        xg_s, x1g_s, x2g_s, acc_s = (chain(n, "sum") for n in ("xg_s", "x1g_s", "x2g_s", "acc_s"))
        qs = chain("qs", "ps hi lo")
        sc0 = [chain(f"sc0_{h}", "ps max negmax exp") for h in range(H0)]
        pt0 = [chain(f"pt0_{h}", "ps hi lo") for h in range(H0)]
        pv0 = chain("pv0", "ps recip norm")
        oTs = chain("oTs", "ps hi lo")
        wo_s = chain("wo_s", "ps x1")
        f0_s = chain("f0_s", "ps x2")
        qps = chain("qps", "ps hi lo c")
        sc1 = chain("sc1", "ps max max_c bias exp")
        rr1_s = chain("rr1_s", "recip gated")
        pt1 = chain("pt1", "ps hi lo")
        zs = chain("zs", "ps hi lo stack")
        o1_s = chain("o1_s", "ps x3")
        qk_s = chain("qk_s", "ps qhi khi qlo klo")
        vg_s = chain("vg_s", "ps vhi vlo max negmax exp")
        gate_s = chain("gate_s", "top index indexf pick0 pick1 comb recip bias scaled")
        sc2 = [chain(f"sc2_{c}", "half ps max_a max_b negmax exp") for c in range(2)]
        moe = [chain(f"moe{j}", "ps even odd") for j in range(NG)]
        moe_sum = [chain(f"moe_sum{j}", "even odd") for j in range(NG)]
        pt2 = [chain(f"pt2_{j}", "ps hi lo") for j in range(NG)]
        pv2 = chain("pv2", "ps recip norm")
        cT_s = chain("cT_s", "ps copy")
        cb_s = chain("cb_s", "ps sum")
        fin = chain("fin", "sum")

        block = ctx.enter_context(nc.Block())

        def iterations(eng, body):
            def at(i):
                return [i - s if 0 <= i - s < NB else None for s in range(4)]
            for i in range(PEEL):
                body(*at(i))
            with eng.Fori(PEEL, NB) as i:
                body(i, i - 1, i - 2, i - 3)
            for i in range(NB, NB + 3):
                body(*at(i))

        @block.sync
        def _(sp):
            sp.dma_start(cst[:], consts).then_inc(loads[0], DMA)
            sp.dma_start(gate_in[:], gates).then_inc(loads[0], DMA)
            sp.dma_start(brow[:], bias_rows).then_inc(loads[0], DMA)

            def load_ctx(b):
                if past(b - 1):
                    sp.wait_ge(kvT[1].sem, kvT[1].after("ps", b - 1))
                if past(b - 1):
                    sp.wait_ge(kvn_split.sem, kvn_split.after("scaled", b - 1))
                sp.dma_start(cin[:], ctx_dup[b]).then_inc(ctx_in.sem, DMA)

            def load_x(b):
                if past(b - 1):
                    sp.wait_ge(xg_s.sem, xg_s.after("sum", b - 1))
                if past(b - 1):
                    sp.wait_ge(ln[0].sem, ln[0].after("xn", b - 1))
                sp.dma_start(xin[:], x[b]).then_inc(x_in.sem, DMA)

            load_ctx(0)
            sp.dma_start(lin[:], w_lin).then_inc(loads[1], DMA)
            for t, w in ((ldT, lora_downT), (dax, down_aux), (luT, lora_upT), (uaT, up_auxT)):
                sp.dma_start(t[:], w).then_inc(loads[2], DMA)
            for t, w in ((l1q, w_l1qT), (l1k, w_l1kT), (l1b, b_l1q)):
                sp.dma_start(t[:], w).then_inc(loads[3], DMA)
            for t, w in ((wqk, w_qk), (wvg, w_vg), (bex, b_exp)):
                sp.dma_start(t[:], w).then_inc(loads[4], DMA)
            sp.dma_start(stack_f[:, D + 1:NST], b_stack).then_inc(loads[4], DMA)
            sp.dma_start(wex[:], w_exp).then_inc(loads[5], DMA)

            def body(a, b, c, d, more):
                if a is not None:
                    load_x(a)
                    if more:
                        load_ctx(a + 1)
                if b is not None:
                    if past(b - 1):
                        sp.wait_ge(zs.sem, zs.after("ps", b - 1))
                    sp.wait_ge(copyAB.sem, copyAB.after("c", b))
                    sp.dma_start(kv[2][:], kv[1][:]).then_inc(copyBC.sem, DMA)
                if a is not None:
                    sp.wait_ge(kvT[1].sem, kvT[1].after("lo", a))
                    sp.wait_ge(kvn_split.sem, kvn_split.after("lo", a))
                    if past(a - 1):
                        sp.wait_ge(copyBC.sem, copyBC.after("c", a - 1))
                    sp.dma_start(kv[1][:], kv[0][:]).then_inc(copyAB.sem, DMA)
                if d is not None:
                    sp.wait_ge(fin.sem, fin.after("sum", d))
                    sp.dma_start(out[d], xout[:]).then_inc(stored.sem, DMA)

            def at(i):
                return [i - s if 0 <= i - s < NB else None for s in range(4)]
            for i in range(PEEL):
                body(*at(i), True)
            with sp.Fori(PEEL, NB - 1) as i:
                body(i, i - 1, i - 2, i - 3, True)
            for i in range(NB - 1, NB + 3):
                body(*at(i), False)
            if past(NB - 1):
                sp.wait_ge(stored.sem, stored.after("c", NB - 1))

        @block.tensor
        def _(pe):
            mm = pe.matmul

            def group(o, terms):
                for n, (w, m) in enumerate(terms):
                    last = mm(o, w, m, start=(n == 0), stop=(n == len(terms) - 1))
                return last

            def three(wh, wl, mh, ml):
                return [(wh, mh), (wh, ml), (wl, mh)]

            pe.wait_ge(loads[2], 4 * DMA)
            mm(bank[0][0:RANK, 0:D], ldT[:], dax[:], start=True, stop=True).then_inc(prep_pe, 1)
            pe.wait_ge(prep, 1)
            mm(bank[1][0:UDIM, 0:D], luT[:], t1[:], start=True, stop=True).then_inc(prep_pe, 1)
            pe.wait_ge(prep, 2)
            for c in range(KD):
                last = mm(bank[2][:, c * D:(c + 1) * D], t2[:, c * P:(c + 1) * P], uaT[:], start=True, stop=True)
            last.then_inc(prep_pe, 1)
            pe.wait_ge(loads[3], 3 * DMA)
            for m in range(KD):
                group(bank[3 + m][:, 0:D + 1], [(l1q[:, c, m * P:(m + 1) * P], l1k[:, c, :]) for c in range(KD)])
            group(bank[5][0:2, 0:D + 1], [(l1b[:, c, :], l1k[:, c, :]) for c in range(KD)]).then_inc(prep_pe, 1)
            pe.wait_ge(prep, PREP)
            pe.wait_ge(prep_pool, 7)
            pe.wait_ge(loads[0], 3 * DMA)

            def ctxT(n, a):
                pe.wait_ge(ctx_in.sem, ctx_in.after("c", a))
                if n == 0:
                    if past(a - 1):
                        pe.wait_ge(vproj[1].sem, vproj[1].after("lo", a - 1))
                else:
                    pe.wait_ge(kvT[0].sem, kvT[0].after("lo", a))
                for c in range(NKC):
                    last = pe.transpose(bank[0][:, c * LKP:(c + 1) * LKP], cin[:, c, n * P:(n + 1) * P],
                                        ident[0:LKP, 0:LKP])
                last.then_inc(kvT[n].sem, 1)

            def kv_terms(w, cols, keys, stationary_w):
                wh, wl = lin_hi[:, w, :, cols], lin_lo[:, w, :, cols]
                xh, xl, xs = kvT0_hi(0)[:, keys], kvT0_lo(0)[:, keys], kvT1(0)[:, keys]
                terms = [(wh[:, 0], xh), (wh[:, 0], xl), (wl[:, 0], xh), (wh[:, 1], xs), (wl[:, 1], xs)]
                return terms if stationary_w else [(m, w) for w, m in terms]

            def project_k(m, a):
                if m == 0:
                    pe.wait_ge(kvT[1].sem, kvT[1].after("lo", a))
                else:
                    pe.wait_ge(kproj[0].sem, kproj[0].after("lo", a))
                group(bank[0][:, 0:LK], kv_terms(WK, slice(m * P, (m + 1) * P), slice(0, LK), True))\
                    .then_inc(kproj[m].sem, 1)

            def project_v(n, a):
                before = kproj[1] if n == 0 else vproj[0]
                pe.wait_ge(before.sem, before.after("lo", a))
                for k, c in enumerate([(0, 1), (2,)][n]):
                    last = group(bank[0][0:LKP, k * D:(k + 1) * D],
                                 kv_terms(WV, slice(0, D), slice(c * LKP, (c + 1) * LKP), False))
                last.then_inc(vproj[n].sem, 1)

            def norm_T(n, b, bk, free, step, fb):
                pe.wait_ge(ln[n].sem, ln[n].after("xn", b))
                if past(fb):
                    pe.wait_ge(free.sem, free.after(step, fb))
                for c in range(KD):
                    last = pe.transpose(bank[bk][:, c * LQ:(c + 1) * LQ], xn[n][:, c * P:(c + 1) * P],
                                        ident[0:LQ, 0:LQ])
                last.then_inc(xTs[n].sem, 1)

            def project_q(b):
                pe.wait_ge(xTs[0].sem, xTs[0].after("lo", b))
                if past(b - 1):
                    pe.wait_ge(pv0.sem, pv0.after("norm", b - 1))
                h, l = xT[0]
                for m in range(KD):
                    cols = slice(m * P, (m + 1) * P)
                    last = group(bank[3][:, m * LQ:(m + 1) * LQ], [t for c in range(KD) for t in three(
                        lin_hi[:, WQ, c, cols], lin_lo[:, WQ, c, cols], h[:, c, :], l[:, c, :])])
                last.then_inc(qs.sem, 1)

            S_BANK = [4, 2, 3, 4]

            def scores0(h, b):
                pe.wait_ge(qs.sem, qs.after("lo", b))
                pe.wait_ge(kproj[1].sem, kproj[1].after("lo", b))
                if h == 0:
                    if past(b - 1):
                        pe.wait_ge(oTs.sem, oTs.after("lo", b - 1))
                if h == 3:
                    pe.wait_ge(sc0[0].sem, sc0[0].after("exp", b))
                r, c = slice(h % 2 * HD0, h % 2 * HD0 + HD0), h // 2
                group(bank[S_BANK[h]][0:LQ, 0:LK],
                      three(q_hi[r, c, :], q_lo[r, c, :], k_hi[r, c, :], k_lo[r, c, :])).then_inc(sc0[h].sem, 1)

            T_BANK = [2, 3, 4, 2]

            def probs0_T(h, b):
                pe.wait_ge(sc0[h].sem, sc0[h].after("exp", b))
                if h < 3:
                    pe.wait_ge(sc0[h + 1].sem, sc0[h + 1].after("exp", b))
                else:
                    pe.wait_ge(pt0[0].sem, pt0[0].after("lo", b))
                for c in range(NKC):
                    last = pe.transpose(bank[T_BANK[h]][0:LKP, c * LQ:(c + 1) * LQ], p0[:, h, c * LKP:(c + 1) * LKP],
                                        ident[0:LQ, 0:LQ])
                last.then_inc(pt0[h].sem, 1)

            def values0(b):
                pe.wait_ge(pt0[3].sem, pt0[3].after("lo", b))
                pe.wait_ge(vproj[1].sem, vproj[1].after("lo", b))
                for h in range(H0):
                    last = group(bank[3][:, h * (HD0 + 1):(h + 1) * (HD0 + 1)], [t for c in range(NKC) for t in three(
                        p0T_hi[:, h, c, :], p0T_lo[:, h, c, :], v_hi[:, c, h, :], v_lo[:, c, h, :])])
                last.then_inc(pv0.sem, 1)

            def out0_T(b):
                pe.wait_ge(pv0.sem, pv0.after("norm", b))
                pe.wait_ge(pt0[2].sem, pt0[2].after("lo", b))
                for c in range(KD):
                    last = pe.transpose(bank[4][:, c * LQ:(c + 1) * LQ], o0[:, c * P:(c + 1) * P], ident[0:LQ, 0:LQ])
                last.then_inc(oTs.sem, 1)

            def project_o(b):
                pe.wait_ge(oTs.sem, oTs.after("lo", b))
                group(bank[2][0:LQ, 0:D], [t for c in range(KD) for t in three(
                    oT_hi[:, c, :], oT_lo[:, c, :], lin_hi[:, WO, c, :], lin_lo[:, WO, c, :])]).then_inc(wo_s.sem, 1)

            def ffn0(c_):
                pe.wait_ge(xTs[1].sem, xTs[1].after("lo", c_))
                h, l = xT[1]
                group(bank[1][0:LQ, 0:D], [t for c in range(KD) for t in three(
                    h[:, c, :], l[:, c, :], lin_hi[:, WF, c, :], lin_lo[:, WF, c, :])]).then_inc(f0_s.sem, 1)

            def query_keys(c_):
                pe.wait_ge(xTs[2].sem, xTs[2].after("lo", c_))
                h, l = xT[2]
                for m in range(KD):
                    cols = slice(m * P, (m + 1) * P)
                    group(bank[1][:, m * LQ:(m + 1) * LQ], [t for c in range(KD) for t in three(
                        A_hi[:, c, cols], A_lo[:, c, cols], h[:, c, :], l[:, c, :])] + [(b_A[:, cols], ones16[:])])
                group(bank[1][0:LQ, KD * LQ:KD * LQ + 1], [t for c in range(KD) for t in three(
                    h[:, c, :], l[:, c, :], A_hi[:, c, D:D + 1], A_lo[:, c, D:D + 1])] + [(ones16[:], b_A[:, D:D + 1])])\
                    .then_inc(qps.sem, 1)

            def scores1(c_):
                pe.wait_ge(qps.sem, qps.after("c", c_))
                pe.wait_ge(copyBC.sem, copyBC.after("c", c_))
                group(bank[1][0:LQ, 0:LK],
                      [(qp_hi[:, 0, :], kvT0_hi(2)), (qp_hi[:, 0, :], kvT0_lo(2)), (qp_lo[:, 0, :], kvT0_hi(2)),
                       (qp_hi[:, 1, :], kvT1(2)), (qp_lo[:, 1, :], kvT1(2))]).then_inc(sc1.sem, 1)

            def probs1_T(c_):
                pe.wait_ge(sc1.sem, sc1.after("exp", c_))
                for c in range(NKC):
                    last = pe.transpose(bank[1][0:LKP, c * LQ:(c + 1) * LQ], p1[:, c * LKP:(c + 1) * LKP],
                                        ident[0:LQ, 0:LQ])
                last.then_inc(pt1.sem, 1)

            def sums1(c_):
                pe.wait_ge(pt1.sem, pt1.after("lo", c_))
                for m in range(KD):
                    cols = slice(m * P, (m + 1) * P)
                    last = group(bank[1][:, m * LQ:(m + 1) * LQ], [t for c in range(NKC) for t in three(
                        kvn(2, 0)[:, c, cols], kvn(2, 1)[:, c, cols], p1T_hi[:, c, :], p1T_lo[:, c, :])])
                last.then_inc(zs.sem, 1)

            def out1(c_):
                pe.wait_ge(zs.sem, zs.after("stack", c_))
                h, l = lin_hi[:, WV1], lin_lo[:, WV1]
                group(bank[1][0:LQ, 0:D], [(z_hi[:, 0, :], h[:, 0, :]), (z_hi[:, 0, :], l[:, 0, :]), (z_lo[:], h[:, 0, :]),
                                           (z_hi[:, 1, :], h[:, 1, :]), (z_hi[:, 1, :], l[:, 1, :])])\
                    .then_inc(o1_s.sem, 1)

            def project_qk(d):
                pe.wait_ge(xTs[3].sem, xTs[3].after("lo", d))
                if past(d - 1):
                    pe.wait_ge(cb_s.sem, cb_s.after("sum", d - 1))
                h, l = xT[3]
                for m in range(4):
                    cols = slice(m * P, (m + 1) * P)
                    last = group(bank[6][:, m * LQ:(m + 1) * LQ], [t for c in range(KD) for t in three(
                        wqk_hi[:, c, cols], wqk_lo[:, c, cols], h[:, c, :], l[:, c, :])] + [(b_qk[:, cols], ones16[:])])
                last.then_inc(qk_s.sem, 1)

            def project_vg(d):
                if past(d - 1):
                    pe.wait_ge(moe[NG - 1].sem, moe[NG - 1].after("odd", d - 1))
                h, l = xT[3]
                group(bank[7][0:LQ, 0:NVG], [t for c in range(KD) for t in three(
                    h[:, c, :], l[:, c, :], wvg_hi[:, c, :], wvg_lo[:, c, :])] + [(ones16[:], b_vg)]).then_inc(vg_s.sem, 1)

            def scores2(c, half, d):
                if half == 1:
                    pe.wait_ge(sc2[c].sem, sc2[c].after("half", d))
                elif c == 0:
                    pe.wait_ge(qk_s.sem, qk_s.after("klo", d))
                else:
                    pe.wait_ge(sc2[0].sem, sc2[0].after("exp", d))
                for n in (2 * half, 2 * half + 1):
                    r = slice(32 * n, 32 * n + 32)
                    o = bank[5 + n % 2][0:LQ, n // 2 * 2 * LQ:(n // 2 + 1) * 2 * LQ]
                    last = group(o, three(q2_hi[r, c, :], q2_lo[r, c, :],
                                          k2_hi[r, c].rearrange("p s q -> p (s q)"),
                                          k2_lo[r, c].rearrange("p s q -> p (s q)")))
                last.then_inc(sc2[c].sem, 1)

            def experts(j, d):
                if j == 0:
                    pe.wait_ge(vg_s.sem, vg_s.after("exp", d))
                else:
                    pe.wait_ge(moe[j - 1].sem, moe[j - 1].after("odd", d))
                h, l = xT[3]
                cols = slice(2 * j, 2 * j + 2)
                group(bank[7][0:LQ, 0:2 * D], [t for c in range(KD) for t in three(
                    h[:, c, :], l[:, c, :], wex_hi[:, c, cols].rearrange("p e n -> p (e n)"),
                    wex_lo[:, c, cols].rearrange("p e n -> p (e n)"))]).then_inc(moe[j].sem, 1)

            def probs2_T(j, d):
                pe.wait_ge(sc2[1].sem, sc2[1].after("exp", d))
                if j >= 2:
                    pe.wait_ge(pt2[j - 2].sem, pt2[j - 2].after("lo", d))
                for s in range(HG):
                    last = pe.transpose(bank[5 + j % 2][0:LQ, s * LQ:(s + 1) * LQ], p2[:, HG * j + s, :],
                                        ident[0:LQ, 0:LQ])
                last.then_inc(pt2[j].sem, 1)

            def values2(d):
                pe.wait_ge(pt2[3].sem, pt2[3].after("lo", d))
                W = HD1 + 1
                for s in range(H1):
                    h = slot_head(s)
                    last = group(bank[5][:, h * W:(h + 1) * W],
                                 three(p2T_hi[:, s, :], p2T_lo[:, s, :], v2_hi[:, h, :], v2_lo[:, h, :]))
                last.then_inc(pv2.sem, 1)

            def combine_T(d):
                pe.wait_ge(gate_s.sem, gate_s.after("bias", d))
                pe.wait_ge(pt2[3].sem, pt2[3].after("lo", d))
                pe.transpose(bank[6][0:E, 0:LQ], cgb[:], ident[0:LQ, 0:LQ]).then_inc(cT_s.sem, 1)

            def expert_bias(d):
                pe.wait_ge(cT_s.sem, cT_s.after("copy", d))
                mm(bank[6][0:LQ, 0:D], cT[:], bex[:], start=True, stop=True).then_inc(cb_s.sem, 1)

            def body(a, b, c, d):
                A, B, C, DD = (v is not None for v in (a, b, c, d))
                if B: project_k(1, b)
                if DD: norm_T(3, d, 5, pv2, "norm", d - 1)
                if B: project_q(b)
                if C: norm_T(1, c, 1, o1_s, "x3", c - 1)
                if B: project_v(0, b)
                if C: ffn0(c)
                if DD: project_qk(d)
                if B: scores0(0, b)
                if B: scores0(1, b)
                if B: project_v(1, b)
                if DD: project_vg(d)
                if B: scores0(2, b)
                if C: norm_T(2, c, 1, f0_s, "x2", c)
                if DD: scores2(0, 0, d)
                if DD: scores2(0, 1, d)
                if B: scores0(3, b)
                if C: query_keys(c)
                if DD: experts(0, d)
                if C: scores1(c)
                if B: probs0_T(0, b)
                if DD: scores2(1, 0, d)
                if B: probs0_T(1, b)
                if A: ctxT(0, a)
                if DD: scores2(1, 1, d)
                if C: probs1_T(c)
                if DD: experts(1, d)
                if B: probs0_T(2, b)
                if B: probs0_T(3, b)
                if C: sums1(c)
                if DD: experts(2, d)
                if B: values0(b)
                if DD: probs2_T(0, d)
                if DD: probs2_T(1, d)
                if C: out1(c)
                if A: ctxT(1, a)
                if B: out0_T(b)
                if DD: experts(3, d)
                if B: project_o(b)
                if DD: probs2_T(2, d)
                if DD: probs2_T(3, d)
                if A: project_k(0, a)
                if A: norm_T(0, a, 4, oTs, "lo", a - 1)
                if DD: combine_T(d)
                if DD: values2(d)
                if DD: expert_bias(d)

            iterations(pe, body)

        @block.scalar
        def _(act):
            act.wait_ge(loads[0], 3 * DMA)
            act.activation(th[:], gate_in[:], ACT.Tanh).then_inc(prep_act, 1)

            def hi(ch, step, b, dst, src, scale, free, fstep, fb):
                act.wait_ge(ch.sem, ch.after(step, b))
                if past(fb):
                    act.wait_ge(free.sem, free.after(fstep, fb))
                act.activation(dst, src, ACT.Copy, scale=scale).then_inc(ch.sem, 1)

            def cols(n, k, w, rows=P):
                return bank[n][0:rows, 0:k * w].rearrange("p (k w) -> p k w", k=k)

            def ctxT_hi(n, a):
                if past(a - 1):
                    act.wait_ge(copyAB.sem, copyAB.after("c", a - 1))
                hi(kvT[n], "ps", a, (kvT0_hi(0), kvT1(0))[n], bank[0][:, 0:LK], SX, vproj[1], "ps", a - 1)

            def k_hi_part(m, a):
                hi(kproj[m], "ps", a, k_hi[:, m, :], bank[0][:, 0:LK], 1 / SW, sc0[3], "ps", a - 1)

            def v_hi_part(n, a):
                cs = [slice(0, 2), slice(2, 3)][n]
                k = cs.stop - cs.start
                act.wait_ge(vproj[n].sem, vproj[n].after("ps", a))
                if past(a - 1):
                    act.wait_ge(pv0.sem, pv0.after("ps", a - 1))
                act.activation(v_hi[:, cs, :, 0:HD0], cols(0, k, D, LKP).rearrange("p c (h e) -> p c h e", h=H0),
                               ACT.Copy, scale=1 / SW).then_inc(vproj[n].sem, 1)

            def exp0(h, b):
                act.wait_ge(sc0[h].sem, sc0[h].after("negmax", b))
                if past(b - 1):
                    act.wait_ge(pt0[h].sem, pt0[h].after("ps", b - 1))
                act.activation(p0[:, h, :], bank[[4, 2, 3, 4][h]][0:LQ, 0:LK], ACT.Exp, bias=nb0[:, h:h + 1],
                               scale=HD0 ** -0.5 / SX ** 2).then_inc(sc0[h].sem, 1)

            def probs0_hi(h, b):
                hi(pt0[h], "ps", b, p0T_hi[:, h, :, 0:LQ], cols([2, 3, 4, 2][h], NKC, LQ, LKP), SP, pv0, "ps", b - 1)

            def exp1(c):
                act.wait_ge(sc1.sem, sc1.after("bias", c))
                if past(c - 1):
                    act.wait_ge(pt1.sem, pt1.after("ps", c - 1))
                if past(c - 1):
                    act.wait_ge(rr1_s.sem, rr1_s.after("recip", c - 1))
                act.activation(p1[:], bank[1][0:LQ, 0:LK], ACT.Exp, bias=nb1[:], scale=SX ** -2, accum_out=rs1[:])\
                    .then_inc(sc1.sem, 1)

            def qk_hi(d):
                hi(qk_s, "ps", d, q2_hi[:], cols(6, 2, LQ), 1 / SW, sc2[1], "ps", d - 1)
                for s in range(2):
                    last = act.activation(k2_hi[:, :, s, :], bank[6][:, 2 * LQ:4 * LQ].rearrange("p (k w) -> p k w", k=2),
                                          ACT.Identity, scale=parity[:, s:s + 1])
                last.then_inc(qk_s.sem, 1)

            def v2_hi_part(d):
                act.wait_ge(vg_s.sem, vg_s.after("ps", d))
                if past(d - 1):
                    act.wait_ge(pv2.sem, pv2.after("ps", d - 1))
                act.activation(v2_hi[:, :, 0:HD1], bank[7][0:LQ, 0:D].rearrange("p (h e) -> p h e", h=H1), ACT.Copy,
                               scale=1 / SW).then_inc(vg_s.sem, 1)

            def gate_exp(d):
                act.wait_ge(vg_s.sem, vg_s.after("negmax", d))
                if past(d - 1):
                    act.wait_ge(gate_s.sem, gate_s.after("recip", d - 1))
                act.activation(eg[:], bank[7][0:LQ, D:D + E], ACT.Exp, bias=ng[:], scale=1 / (SX * SW), accum_out=sg[:])\
                    .then_inc(vg_s.sem, 1)

            def exp2(c, d):
                act.wait_ge(sc2[c].sem, sc2[c].after("negmax", d))
                for j in (2 * c, 2 * c + 1):
                    if past(d - 1):
                        act.wait_ge(pt2[j].sem, pt2[j].after("ps", d - 1))
                for s in range(8):
                    last = act.activation(p2[:, 8 * c + s, :], bank[5 + s // 4][0:LQ, s % 4 * LQ:(s % 4 + 1) * LQ],
                                          ACT.Exp, bias=nb2[:, 8 * c + s:8 * c + s + 1], scale=HD1 ** -0.5 / SX ** 2)
                last.then_inc(sc2[c].sem, 1)

            def weigh_experts(j, d):
                act.wait_ge(moe[j].sem, moe[j].after("ps", d))
                act.wait_ge(gate_s.sem, gate_s.after("scaled", d))
                for n in range(2):
                    e = 2 * j + n
                    if past(d - 1):
                        act.wait_ge(moe_sum[j].sem, moe_sum[j].after("odd", d - 1))
                    act.activation(part[:, e, :], bank[7][0:LQ, n * D:(n + 1) * D], ACT.Identity, scale=cgS[:, e:e + 1])\
                        .then_inc(moe[j].sem, 1)

            def probs2_hi(j, d):
                hi(pt2[j], "ps", d, p2T_hi[:, HG * j:HG * j + HG, 0:LQ], cols(5 + j % 2, HG, LQ, LQ), SP, pv2, "ps", d - 1)

            def body(a, b, c, d):
                A, B, C, DD = (v is not None for v in (a, b, c, d))
                if B: k_hi_part(1, b)
                if B: hi(qs, "ps", b, q_hi[:], cols(3, KD, LQ), 1 / SW, sc0[3], "ps", b - 1)
                if C: hi(xTs[1], "ps", c, xT[1][0][:], cols(1, KD, LQ), SX, f0_s, "ps", c - 1)
                if DD: hi(xTs[3], "ps", d, xT[3][0][:], cols(5, KD, LQ), SX, moe[NG - 1], "ps", d - 1)
                if B: v_hi_part(0, b)
                if DD: qk_hi(d)
                if B: exp0(0, b)
                if DD: v2_hi_part(d)
                if B: v_hi_part(1, b)
                if C: hi(xTs[2], "ps", c, xT[2][0][:], cols(1, KD, LQ), SX, qps, "ps", c - 1)
                if DD: gate_exp(d)
                if B: exp0(1, b)
                if C: hi(qps, "ps", c, qp_hi[:], cols(1, KD, LQ), 1 / SW, sc1, "ps", c - 1)
                if B: exp0(2, b)
                if DD: exp2(0, d)
                if DD: weigh_experts(0, d)
                if B: exp0(3, b)
                if C: exp1(c)
                if B: probs0_hi(0, b)
                if B: probs0_hi(1, b)
                if C: hi(pt1, "ps", c, p1T_hi[:], cols(1, NKC, LQ, LKP), SP, zs, "ps", c - 1)
                if A: ctxT_hi(0, a)
                if B: probs0_hi(2, b)
                if DD: weigh_experts(1, d)
                if B: probs0_hi(3, b)
                if DD: exp2(1, d)
                if C: hi(zs, "ps", c, z_hi[:], cols(1, KD, LQ), SZ / (SX * SP), o1_s, "ps", c - 1)
                if DD: weigh_experts(2, d)
                if DD: probs2_hi(0, d)
                if DD: probs2_hi(1, d)
                if B: hi(oTs, "ps", b, oT_hi[:], cols(4, KD, LQ), 1.0, wo_s, "ps", b - 1)
                if A: ctxT_hi(1, a)
                if DD: probs2_hi(2, d)
                if DD: probs2_hi(3, d)
                if A: k_hi_part(0, a)
                if A: hi(xTs[0], "ps", a, xT[0][0][:], cols(4, KD, LQ), SX, qs, "ps", a - 1)
                if DD: weigh_experts(3, d)

            iterations(act, body)

        @block.vector
        def _(dve):
            ts, stt, tt = dve.tensor_scalar, dve.scalar_tensor_tensor, dve.tensor_tensor
            done = [0]

            def prepared(ins):
                ins.then_inc(prep, 1)
                done[0] += 1
                dve.wait_ge(prep, done[0])

            def split_w(dh, dl, src, scale=SW):
                prepared(ts(dh, src, scale, None, ALU.mult))
                prepared(stt(dl, src, scale, dh, ALU.mult, ALU.subtract))

            dve.wait_ge(prep_pe, 1)
            prepared(dve.tensor_copy(t1[:], bank[0][0:RANK, 0:D]))
            dve.wait_ge(prep_pe, 2)
            prepared(dve.tensor_copy(t2[:], bank[1][0:UDIM, 0:D]))
            dve.wait_ge(loads[1], DMA)
            dve.wait_ge(prep_pe, 3)
            prepared(tt(lin[:, WF], lin[:, WF], bank[2][:, 0:2 * D].rearrange("p (k n) -> p k n", k=KD), ALU.add))
            split_w(lin_hi[:], lin_lo[:], lin[:])
            dve.wait_ge(prep_pe, 4)
            for m in range(KD):
                split_w(A_hi[:, m, :], A_lo[:, m, :], bank[3 + m][:, 0:D + 1])
            prepared(ts(stack_f[:, 0:D + 1], bank[5][0:2, 0:D + 1], 1.0, None, ALU.mult))
            dve.wait_ge(loads[4], 4 * DMA)
            dve.wait_ge(loads[0], 3 * DMA)
            prepared(ts(stack_f[:], stack_f[:], SW, None, ALU.mult))
            prepared(dve.tensor_copy(stack_h[:], stack_f[:]))
            prepared(stt(stack[:], stack_h[:], keep_hi_row, stack_f[:], ALU.mult, ALU.add))
            split_w(wqk_hi[:], wqk_lo[:], wqk[:])
            split_w(wvg_hi[:], wvg_lo[:], wvg[:])
            dve.wait_ge(loads[5], DMA)
            split_w(wex_hi[:], wex_lo[:], wex[:])
            prepared(dve.memset(v_hi[:, :, :, HD0:HD0 + 1], 1.0))
            prepared(dve.memset(v_lo[:, :, :, HD0:HD0 + 1], 0.0))
            prepared(dve.memset(v2_hi[:, :, HD1:HD1 + 1], 1.0))
            prepared(dve.memset(v2_lo[:, :, HD1:HD1 + 1], 0.0))
            prepared(dve.memset(ones16[:], SX))
            dve.wait_ge(prep_act, 1)
            for n, s in enumerate((1 / (SX * SW), 1 / (SX * SW), 1 / (SZ * SW), 1 / (SX * SW), 1.0, 1 / SX)):
                prepared(ts(gsc[:, n:n + 1], th[:, min(n, 3):min(n, 3) + 1], s, None, ALU.mult))
            for n in range(3):
                prepared(ts(gbrow[:, n, :], brow[:, n, :], th[:, n:n + 1], None, ALU.mult))
            assert done[0] == PREP, done[0]
            dve.wait_ge(prep_pool, 7)

            def cols(n, k, w, rows=P):
                return bank[n][0:rows, 0:k * w].rearrange("p (k w) -> p k w", k=k)

            def lo(ch, b, dst, src, scale, dst_hi, free, fstep, fb):
                dve.wait_ge(ch.sem, ch.after("hi", b))
                if past(fb):
                    dve.wait_ge(free.sem, free.after(fstep, fb))
                stt(dst, src, scale, dst_hi, ALU.mult, ALU.subtract).then_inc(ch.sem, 1)

            def stats(n, src, ready, step, b):
                dve.wait_ge(ready.sem, ready.after(step, b))
                if past(b - 1):
                    dve.wait_ge(ln[n].sem, ln[n].after("mean_var", b - 1))
                dve.bn_stats(ln_st[n][:], src[:]).then_inc(ln[n].sem, 1)

            def mean_var(n, b):
                dve.wait_ge(ln[n].sem, ln[n].after("stats", b))
                dve.nop(nofuse=True)
                dve.bn_aggr(ln_mv[n][:], ln_st[n][:]).then_inc(ln[n].sem, 1)

            def ctxT_lo(n, a):
                if past(a - 1):
                    dve.wait_ge(copyAB.sem, copyAB.after("c", a - 1))
                if n == 0:
                    lo(kvT[0], a, kvT0_lo(0), bank[0][:, 0:LK], SX, kvT0_hi(0), vproj[1], "ps", a - 1)
                else:
                    r = slice(64, P)
                    lo(kvT[1], a, kvT1(0)[r], bank[0][r, 0:LK], SX, kvT1(0)[r], vproj[1], "ps", a - 1)

            def v_lo_part(n, a):
                cs = [slice(0, 2), slice(2, 3)][n]
                k = cs.stop - cs.start
                dve.wait_ge(vproj[n].sem, vproj[n].after("hi", a))
                if past(a - 1):
                    dve.wait_ge(pv0.sem, pv0.after("ps", a - 1))
                for m, c in enumerate(range(cs.start, cs.stop)):
                    last = stt(v_lo[:, c, :, 0:HD0],
                               bank[0][0:LKP, m * D:(m + 1) * D].rearrange("p (h e) -> p h e", h=H0),
                               1 / SW, v_hi[:, c, :, 0:HD0], ALU.mult, ALU.subtract)
                last.then_inc(vproj[n].sem, 1)

            def max0(h, b):
                dve.wait_ge(sc0[h].sem, sc0[h].after("ps", b))
                if past(b - 1):
                    dve.wait_ge(sc0[h].sem, sc0[h].after("negmax", b - 1))
                dve.tensor_reduce(mx0[:, h:h + 1], bank[[4, 2, 3, 4][h]][0:LQ, 0:LK], AX.X, ALU.max)\
                    .then_inc(sc0[h].sem, 1)

            def negmax0(h, b):
                dve.wait_ge(sc0[h].sem, sc0[h].after("max", b))
                if past(b - 1):
                    dve.wait_ge(sc0[h].sem, sc0[h].after("exp", b - 1))
                ts(nb0[:, h:h + 1], mx0[:, h:h + 1], -(HD0 ** -0.5) / SX ** 2, None, ALU.mult).then_inc(sc0[h].sem, 1)

            def probs0_lo(h, b):
                lo(pt0[h], b, p0T_lo[:, h, :, 0:LQ], cols([2, 3, 4, 2][h], NKC, LQ, LKP), SP, p0T_hi[:, h, :, 0:LQ], pv0,
                   "ps", b - 1)

            def norm0(b):
                pv = cols(3, H0, HD0 + 1, LQ)
                dve.wait_ge(pv0.sem, pv0.after("ps", b))
                dve.reciprocal(rec0[:].rearrange("p (h o) -> p h o", o=1), pv[:, :, HD0:HD0 + 1]).then_inc(pv0.sem, 1)
                dve.wait_ge(pv0.sem, pv0.after("recip", b))
                if past(b - 1):
                    dve.wait_ge(oTs.sem, oTs.after("ps", b - 1))
                tt(o0[:].rearrange("p (h e) -> p h e", h=H0), pv[:, :, 0:HD0],
                   rec0[:].rearrange("p (h o) -> p h o", o=1).broadcast_to([LQ, H0, HD0]), ALU.mult)\
                    .then_inc(pv0.sem, 1)

            def residual(ch, step, b, dst, bk, gate, base, base_s, frees):
                dve.wait_ge(ch.sem, ch.after("ps", b))
                dve.wait_ge(base_s.sem, base_s.after("sum", b))
                for f, fs in frees:
                    if past(b - 1):
                        dve.wait_ge(f.sem, f.after(fs, b - 1))
                stt(dst[:], bank[bk][0:LQ, 0:D], gate, base[:], ALU.mult, ALU.add).then_inc(ch.sem, 1)

            def query_const(c):
                dve.wait_ge(qps.sem, qps.after("lo", c))
                if past(c - 1):
                    dve.wait_ge(sc1.sem, sc1.after("bias", c - 1))
                ts(qc[:], bank[1][0:LQ, KD * LQ:KD * LQ + 1], 1 / (SX * SW), None, ALU.mult).then_inc(qps.sem, 1)

            def max1(c):
                dve.wait_ge(sc1.sem, sc1.after("ps", c))
                if past(c - 1):
                    dve.wait_ge(sc1.sem, sc1.after("max_c", c - 1))
                dve.tensor_reduce(mx1[:], bank[1][0:LQ, 0:LK], AX.X, ALU.max).then_inc(sc1.sem, 1)
                dve.wait_ge(sc1.sem, sc1.after("max", c))
                dve.wait_ge(qps.sem, qps.after("c", c))
                stt(mm1[:], mx1[:], SX ** -2, qc[:], ALU.mult, ALU.add).then_inc(sc1.sem, 1)
                dve.wait_ge(sc1.sem, sc1.after("max_c", c))
                tt(nb1[:], qc[:], mm1[:], ALU.subtract).then_inc(sc1.sem, 1)

            def recip1(c):
                dve.wait_ge(sc1.sem, sc1.after("exp", c))
                if past(c - 1):
                    dve.wait_ge(rr1_s.sem, rr1_s.after("gated", c - 1))
                dve.reciprocal(rr1[:], rs1[:]).then_inc(rr1_s.sem, 1)
                dve.wait_ge(rr1_s.sem, rr1_s.after("recip", c))
                if past(c - 1):
                    dve.wait_ge(o1_s.sem, o1_s.after("x3", c - 1))
                ts(gr1[:], rr1[:], gsc[:, 2:3], None, ALU.mult).then_inc(rr1_s.sem, 1)

            def z_parts(c):
                s = SZ / (SX * SP)
                dve.wait_ge(zs.sem, zs.after("hi", c))
                if past(c - 1):
                    dve.wait_ge(o1_s.sem, o1_s.after("ps", c - 1))
                stt(z_lo[:], bank[1][:, 0:LQ], s, z_hi[:, 0, :], ALU.mult, ALU.subtract).then_inc(zs.sem, 1)
                r = slice(64, P)
                stt(z_hi[r, 1, :], bank[1][r, LQ:2 * LQ], s, z_hi[r, 1, :], ALU.mult, ALU.subtract).then_inc(zs.sem, 1)

            def out1_sum(c):
                dve.wait_ge(rr1_s.sem, rr1_s.after("gated", c))
                residual(o1_s, "x3", c, x3, 1, gr1[:, 0:1], x2g, x2g_s, [(ln[3], "xn"), (acc_s, "sum")])

            def qk_lo(d):
                dve.wait_ge(qk_s.sem, qk_s.after("khi", d))
                if past(d - 1):
                    dve.wait_ge(sc2[1].sem, sc2[1].after("ps", d - 1))
                stt(q2_lo[:], cols(6, 2, LQ), 1 / SW, q2_hi[:], ALU.mult, ALU.subtract).then_inc(qk_s.sem, 1)
                for s in range(2):
                    last = stt(k2_lo[:, :, s, :], bank[6][:, 2 * LQ:4 * LQ].rearrange("p (k w) -> p k w", k=2),
                               parity[:, s:s + 1], k2_hi[:, :, s, :], ALU.mult, ALU.subtract)
                last.then_inc(qk_s.sem, 1)

            def v2_lo_part(d):
                dve.wait_ge(vg_s.sem, vg_s.after("vhi", d))
                if past(d - 1):
                    dve.wait_ge(pv2.sem, pv2.after("ps", d - 1))
                stt(v2_lo[:, :, 0:HD1], bank[7][0:LQ, 0:D].rearrange("p (h e) -> p h e", h=H1), 1 / SW,
                    v2_hi[:, :, 0:HD1], ALU.mult, ALU.subtract).then_inc(vg_s.sem, 1)
                if past(d - 1):
                    dve.wait_ge(vg_s.sem, vg_s.after("negmax", d - 1))
                dve.tensor_reduce(mg[:], bank[7][0:LQ, D:D + E], AX.X, ALU.max).then_inc(vg_s.sem, 1)
                dve.wait_ge(vg_s.sem, vg_s.after("max", d))
                if past(d - 1):
                    dve.wait_ge(vg_s.sem, vg_s.after("exp", d - 1))
                ts(ng[:], mg[:], -1 / (SX * SW), None, ALU.mult).then_inc(vg_s.sem, 1)

            def gate_max(d):
                dve.wait_ge(vg_s.sem, vg_s.after("exp", d))
                if past(d - 1):
                    dve.wait_ge(gate_s.sem, gate_s.after("pick1", d - 1))
                dve.nop(nofuse=True)
                dve.max(top[:], eg[:]).then_inc(gate_s.sem, 1)

            def gate_index(d):
                dve.wait_ge(gate_s.sem, gate_s.after("top", d))
                dve.nop(nofuse=True)
                dve.max_index(topi[:], top[:], eg[:]).then_inc(gate_s.sem, 1)

            def gate_indexf(d):
                dve.wait_ge(gate_s.sem, gate_s.after("index", d))
                dve.tensor_copy(topf[:], topi[:, 0:2]).then_inc(gate_s.sem, 1)

            def gate_pick(d):
                dve.wait_ge(gate_s.sem, gate_s.after("indexf", d))
                if past(d - 1):
                    dve.wait_ge(gate_s.sem, gate_s.after("comb", d - 1))
                ts(pick0[:], iota, topf[:, 0:1], top[:, 0:1], ALU.is_equal, ALU.mult).then_inc(gate_s.sem, 1)
                ts(pick1[:], iota, topf[:, 1:2], top[:, 1:2], ALU.is_equal, ALU.mult).then_inc(gate_s.sem, 1)

            def gate_combine(d):
                dve.wait_ge(gate_s.sem, gate_s.after("pick1", d))
                if past(d - 1):
                    dve.wait_ge(gate_s.sem, gate_s.after("scaled", d - 1))
                tt(comb[:], pick0[:], pick1[:], ALU.add).then_inc(gate_s.sem, 1)
                dve.reciprocal(rsg[:], sg[:]).then_inc(gate_s.sem, 1)

            def gate_weights(d):
                dve.wait_ge(gate_s.sem, gate_s.after("recip", d))
                if past(d - 1):
                    dve.wait_ge(cT_s.sem, cT_s.after("ps", d - 1))
                ts(cgb[:], comb[:], rsg[:], gsc[:, 4:5], ALU.mult, ALU.mult).then_inc(gate_s.sem, 1)

            def gate_scaled(d):
                dve.wait_ge(gate_s.sem, gate_s.after("bias", d))
                if past(d - 1):
                    dve.wait_ge(moe[NG - 1].sem, moe[NG - 1].after("odd", d - 1))
                ts(cgS[:], cgb[:], 1 / (SX * SW), None, ALU.mult).then_inc(gate_s.sem, 1)

            def max2(c, d):
                dve.wait_ge(sc2[c].sem, sc2[c].after("ps", d))
                if past(d - 1):
                    dve.wait_ge(sc2[c].sem, sc2[c].after("negmax", d - 1))
                for n in range(2):
                    o = 8 * c + 4 * n
                    dve.tensor_reduce(mx2[:, o:o + 4], cols(5 + n, 4, LQ, LQ), AX.X, ALU.max).then_inc(sc2[c].sem, 1)
                dve.wait_ge(sc2[c].sem, sc2[c].after("max_b", d))
                if past(d - 1):
                    dve.wait_ge(sc2[c].sem, sc2[c].after("exp", d - 1))
                ts(nb2[:, 8 * c:8 * c + 8], mx2[:, 8 * c:8 * c + 8], -(HD1 ** -0.5) / SX ** 2, None, ALU.mult)\
                    .then_inc(sc2[c].sem, 1)

            def probs2_lo(j, d):
                r = slice(HG * j, HG * j + HG)
                lo(pt2[j], d, p2T_lo[:, r, 0:LQ], cols(5 + j % 2, HG, LQ, LQ), SP, p2T_hi[:, r, 0:LQ], pv2, "ps", d - 1)

            def norm2(d):
                pv = cols(5, H1, HD1 + 1, LQ)
                dve.wait_ge(pv2.sem, pv2.after("ps", d))
                dve.reciprocal(rec2[:].rearrange("p (h o) -> p h o", o=1), pv[:, :, HD1:HD1 + 1]).then_inc(pv2.sem, 1)
                dve.wait_ge(pv2.sem, pv2.after("recip", d))
                if past(d - 1):
                    dve.wait_ge(fin.sem, fin.after("sum", d - 1))
                tt(o2[:].rearrange("p (h e) -> p h e", h=H1), pv[:, :, 0:HD1],
                   rec2[:].rearrange("p (h o) -> p h o", o=1).broadcast_to([LQ, H1, HD1]), ALU.mult)\
                    .then_inc(pv2.sem, 1)

            def combine_copy(d):
                dve.wait_ge(cT_s.sem, cT_s.after("ps", d))
                dve.tensor_copy(cT[:], bank[6][0:E, 0:LQ]).then_inc(cT_s.sem, 1)

            def add_bias2(d):
                dve.wait_ge(cb_s.sem, cb_s.after("ps", d))
                dve.wait_ge(pv2.sem, pv2.after("norm", d))
                stt(o2[:], o2[:], gsc[:, 5:6], bank[6][0:LQ, 0:D], ALU.mult, ALU.add).then_inc(cb_s.sem, 1)

            def body(a, b, c, d):
                A, B, C, DD = (v is not None for v in (a, b, c, d))
                if B: lo(kproj[1], b, k_lo[:, 1, :], bank[0][:, 0:LK], 1 / SW, k_hi[:, 1, :], sc0[3], "ps", b - 1)
                if DD: lo(xTs[3], d, xT[3][1][:], cols(5, KD, LQ), SX, xT[3][0][:], moe[NG - 1], "ps", d - 1)
                if C: lo(xTs[1], c, xT[1][1][:], cols(1, KD, LQ), SX, xT[1][0][:], f0_s, "ps", c - 1)
                if B: lo(qs, b, q_lo[:], cols(3, KD, LQ), 1 / SW, q_hi[:], sc0[3], "ps", b - 1)
                if B: v_lo_part(0, b)
                if C: residual(f0_s, "x2", c, x2, 1, gsc[:, 1:2], x1g, x1g_s, [(ln[2], "xn"), (x2g_s, "sum")])
                if C: stats(2, x2, f0_s, "x2", c)
                if C: mean_var(2, c)
                if B: max0(0, b)
                if B: negmax0(0, b)
                if DD: qk_lo(d)
                if B: max0(1, b)
                if DD: v2_lo_part(d)
                if B: negmax0(1, b)
                if C: lo(xTs[2], c, xT[2][1][:], cols(1, KD, LQ), SX, xT[2][0][:], qps, "ps", c - 1)
                if DD: gate_max(d)
                if B: max0(2, b)
                if B: v_lo_part(1, b)
                if DD: gate_index(d)
                if B: negmax0(2, b)
                if DD: gate_indexf(d)
                if DD: max2(0, d)
                if DD: gate_pick(d)
                if C: lo(qps, c, qp_lo[:], cols(1, KD, LQ), 1 / SW, qp_hi[:], sc1, "ps", c - 1)
                if C: query_const(c)
                if DD: gate_combine(d)
                if DD: gate_weights(d)
                if B: max0(3, b)
                if DD: gate_scaled(d)
                if B: negmax0(3, b)
                if C: max1(c)
                if B: probs0_lo(0, b)
                if B: probs0_lo(1, b)
                if C: lo(pt1, c, p1T_lo[:], cols(1, NKC, LQ, LKP), SP, p1T_hi[:], zs, "ps", c - 1)
                if DD: max2(1, d)
                if A: ctxT_lo(0, a)
                if B: probs0_lo(2, b)
                if B: probs0_lo(3, b)
                if A: stats(0, xin, x_in, "x", a)
                if C: recip1(c)
                if C: z_parts(c)
                if A: mean_var(0, a)
                if B: norm0(b)
                if DD: probs2_lo(0, d)
                if DD: probs2_lo(1, d)
                if B: lo(oTs, b, oT_lo[:], cols(4, KD, LQ), 1.0, oT_hi[:], wo_s, "ps", b - 1)
                if C: out1_sum(c)
                if A: ctxT_lo(1, a)
                if C: stats(3, x3, o1_s, "x3", c)
                if B: residual(wo_s, "x1", b, x1, 2, gsc[:, 0:1], xg, xg_s, [(ln[1], "xn"), (x1g_s, "sum")])
                if C: mean_var(3, c)
                if B: stats(1, x1, wo_s, "x1", b)
                if DD: probs2_lo(2, d)
                if B: mean_var(1, b)
                if DD: probs2_lo(3, d)
                if DD: combine_copy(d)
                if A: lo(xTs[0], a, xT[0][1][:], cols(4, KD, LQ), SX, xT[0][0][:], qs, "ps", a - 1)
                if A: lo(kproj[0], a, k_lo[:, 0, :], bank[0][:, 0:LK], 1 / SW, k_hi[:, 0, :], sc0[3], "ps", a - 1)
                if DD: norm2(d)
                if DD: add_bias2(d)

            iterations(dve, body)

        @block.gpsimd
        def _(pool):
            for g in range(3):
                pool.memset(kv[g][:], 0.0).then_inc(prep_pool, 1)
            for t in (p0T_hi, p0T_lo, p2T_hi, p2T_lo):
                pool.memset(t[:], 0.0).then_inc(prep_pool, 1)
            pool.wait_ge(prep, PREP)

            def normalise(n, src, b):
                pool.wait_ge(ln[n].sem, ln[n].after("mean_var", b))
                pool.nop(nofuse=True)
                pool.tensor_scalar(ln_ve[n][:], ln_mv[n][:, 1:2], EPS, None, ALU.add).then_inc(ln[n].sem, 1)
                pool.wait_ge(ln[n].sem, ln[n].after("var_eps", b))
                pool.tensor_tensor(ln_rs[n][:], ln_ve[n][:], minus_half, ALU.pow).then_inc(ln[n].sem, 1)
                pool.wait_ge(ln[n].sem, ln[n].after("rstd", b))
                pool.nop(nofuse=True)
                pool.tensor_scalar(ln_sh[n][:], ln_mv[n][:, 0:1], ln_rs[n][:], -1.0, ALU.mult, ALU.mult).then_inc(ln[n].sem, 1)
                pool.wait_ge(ln[n].sem, ln[n].after("shift", b))
                if past(b - 1):
                    pool.wait_ge(xTs[n].sem, xTs[n].after("ps", b - 1))
                pool.nop(nofuse=True)
                pool.tensor_scalar(xn[n][:], src[:], ln_rs[n][:], ln_sh[n][:], ALU.mult, ALU.add).then_inc(ln[n].sem, 1)

            def add_bias(dst, src, n, ch, b, ready, step, free, fstep):
                pool.wait_ge(ready.sem, ready.after(step, b))
                if past(b - 1):
                    pool.wait_ge(free.sem, free.after(fstep, b - 1))
                pool.tensor_tensor(dst[:], src[:], gbrow[:, n, :], ALU.add).then_inc(ch.sem, 1)

            def split_ctx(a):
                pool.wait_ge(ctx_in.sem, ctx_in.after("c", a))
                if past(a - 1):
                    pool.wait_ge(kvn_split.sem, kvn_split.after("lo", a - 1))
                pool.nop(nofuse=True)
                pool.tensor_scalar(cinS[:], cin[:], SX, 0.0, ALU.mult, ALU.add).then_inc(kvn_split.sem, 1)
                pool.wait_ge(kvn_split.sem, kvn_split.after("scaled", a))
                if past(a - 1):
                    pool.wait_ge(copyAB.sem, copyAB.after("c", a - 1))
                pool.nop(nofuse=True)
                pool.tensor_scalar(kvn(0, 0), cinS[:], 1.0, 0.0, ALU.mult, ALU.add).then_inc(kvn_split.sem, 1)
                pool.wait_ge(kvn_split.sem, kvn_split.after("hi", a))
                pool.tensor_tensor(kvn(0, 1), cinS[:], kvn(0, 0), ALU.subtract).then_inc(kvn_split.sem, 1)

            def start_sum(d):
                pool.wait_ge(o1_s.sem, o1_s.after("x3", d))
                if past(d - 1):
                    pool.wait_ge(fin.sem, fin.after("sum", d - 1))
                pool.nop(nofuse=True)
                pool.tensor_scalar(acc[:], x3[:], 1.0, 0.0, ALU.mult, ALU.add).then_inc(acc_s.sem, 1)

            def add_experts(j, d):
                before = acc_s if j == 0 else moe_sum[j - 1]
                pool.wait_ge(before.sem, before.after("sum" if j == 0 else "odd", d))
                for n, step in enumerate(("even", "odd")):
                    if n:
                        pool.wait_ge(moe_sum[j].sem, moe_sum[j].after("even", d))
                    pool.wait_ge(moe[j].sem, moe[j].after(step, d))
                    pool.tensor_tensor(acc[:], part[:, 2 * j + n, :], acc[:], ALU.add).then_inc(moe_sum[j].sem, 1)

            def finish(d):
                pool.wait_ge(cb_s.sem, cb_s.after("sum", d))
                pool.wait_ge(moe_sum[NG - 1].sem, moe_sum[NG - 1].after("odd", d))
                if past(d - 1):
                    pool.wait_ge(stored.sem, stored.after("c", d - 1))
                pool.tensor_tensor(xout[:], o2[:], acc[:], ALU.add).then_inc(fin.sem, 1)

            def body(a, b, c, d):
                A, B, C, DD = (v is not None for v in (a, b, c, d))
                if DD: start_sum(d)
                if C: normalise(2, x2, c)
                if C: add_bias(x2g, x2, 2, x2g_s, c, f0_s, "x2", o1_s, "x3")
                if A: split_ctx(a)
                if DD: add_experts(0, d)
                if B: add_bias(xg, xin, 0, xg_s, b, x_in, "x", wo_s, "x1")
                if A: normalise(0, xin, a)
                if C: normalise(3, x3, c)
                if B: normalise(1, x1, b)
                if DD: add_experts(1, d)
                if DD: add_experts(2, d)
                if B: add_bias(x1g, x1, 1, x1g_s, b, wo_s, "x1", f0_s, "x2")
                if DD: add_experts(3, d)
                if DD: finish(d)

            iterations(pool, body)


PREP = 33


_OUT = ((32, 112, 256), "float32")


def kernel(x, ctx_768, g_xattn, g_ffn, L0_xattn_Wq, L0_xattn_Wk, L0_xattn_Wv, L0_xattn_Wo, L0_xattn_bo, L0_ffn_W,
           L0_ffn_b, L0_ffn_lora_down, L0_ffn_lora_up, L0_ffn_down_aux, L0_ffn_up_aux, L1_xattn_Wq, L1_xattn_bq,
           L1_xattn_Wk, L1_xattn_bk, L1_xattn_Wv, L1_xattn_bv, L1_ffn_W_qkv, L1_ffn_b_qkv, L1_ffn_W_gate,
           L1_ffn_b_gate, L1_ffn_W_experts, L1_ffn_b_experts):
    import numpy as np
    import concourse.bacc as bacc
    from concourse.bass_utils import run_bass_kernel_spmd

    f = lambda a: np.ascontiguousarray(np.asarray(a))
    B, LQ, D = x.shape
    LK, DK = ctx_768.shape[1:]
    T = 128

    def rows(w):
        return w.reshape(-1, T, w.shape[1]).transpose(1, 0, 2)

    def dup(w):
        return rows(np.concatenate([w[:DK], w[T:DK]], axis=0))

    ctx = np.asarray(ctx_768)
    ctx = np.concatenate([ctx, ctx[:, :, T:DK]], axis=2)
    ctx = ctx.reshape(B, 3, LK // 3, 2 * T).transpose(0, 2, 1, 3)
    E = L1_ffn_W_gate.shape[1]
    consts = np.zeros((T, T + 4 + E), np.float32)
    consts[:, :T] = np.eye(T)
    consts[1, T] = -1.0
    for p in range(T):
        consts[p, T + 1 + p // 16 % 2] = 1.0 / 256
    consts[:, T + 3:T + 3 + E] = np.arange(E)
    consts[:, T + 3 + E] = -0.5
    a = {k: np.asarray(v) for k, v in dict(
        wq=L0_xattn_Wq, wk=L0_xattn_Wk, wv=L0_xattn_Wv, wo=L0_xattn_Wo, wf=L0_ffn_W, l1v=L1_xattn_Wv, l1q=L1_xattn_Wq,
        l1k=L1_xattn_Wk, wqkv=L1_ffn_W_qkv, bqkv=L1_ffn_b_qkv, wg=L1_ffn_W_gate, bg=L1_ffn_b_gate).items()}
    l1kT = a["l1k"].T
    arrays = {
        "x": f(x), "ctx_dup": f(ctx), "consts": consts,
        "gates": f(np.broadcast_to(np.stack([np.asarray(g_xattn)[0], np.asarray(g_ffn)[0], np.asarray(g_xattn)[1],
                                             np.asarray(g_ffn)[1]]), (LQ, 4))),
        "bias_rows": f(np.broadcast_to(np.stack([np.asarray(L0_xattn_bo), np.asarray(L0_ffn_b),
                                                 np.asarray(L1_xattn_bv)]), (LQ, 3, D))),
        "w_lin": f(np.stack([rows(a["wq"].T), dup(a["wk"].T), dup(a["wv"].T), rows(a["wo"].T), rows(a["wf"].T),
                             dup(a["l1v"])], axis=1)),
        "lora_downT": f(np.asarray(L0_ffn_lora_down).T), "down_aux": f(L0_ffn_down_aux),
        "lora_upT": f(np.asarray(L0_ffn_lora_up).T), "up_auxT": f(np.asarray(L0_ffn_up_aux).T),
        "w_l1qT": f(rows(a["l1q"].T)),
        "w_l1kT": f(rows(np.concatenate([l1kT, l1kT[:, T:DK], np.asarray(L1_xattn_bk)[:, None]], axis=1))),
        "b_l1q": f(np.repeat(np.asarray(L1_xattn_bq).reshape(2, T).T[:, :, None], 2, axis=2)),
        "w_qk": f(rows(a["wqkv"][:, :2 * D])),
        "w_vg": f(rows(np.concatenate([a["wqkv"][:, 2 * D:], a["wg"]], axis=1))),
        "b_stack": f(np.broadcast_to(np.concatenate([a["bqkv"], a["bg"]]), (2, 3 * D + E))),
        "w_exp": f(np.asarray(L1_ffn_W_experts).reshape(E, 2, T, D).transpose(2, 1, 0, 3)),
        "b_exp": f(L1_ffn_b_experts),
    }
    nc = bacc.Bacc("TRN2", target_bir_lowering=False, num_devices=1)
    args = {n: nc.dram_tensor("in_" + n, v.shape, mybir.dt.from_np(v.dtype), kind="ExternalInput").ap()
            for n, v in arrays.items()}
    out = nc.dram_tensor("out_x", _OUT[0], F32, kind="ExternalOutput").ap()
    flamingo_kernel(nc, out=out, **args)
    r = run_bass_kernel_spmd(nc, [{"in_" + n: v for n, v in arrays.items()}], core_ids=[0])
    return r.results[0]["out_x"]
```
